# Optimizing a Trainium2 kernel written in Bass

```python
import numpy as np
import jax
import jax.numpy as jnp

def _softmax(x, axis=-1):
    return jax.nn.softmax(x, axis=axis)

def _gelu(x):
    return jax.nn.gelu(x, approximate=True)

def _silu(x):
    return jax.nn.silu(x)

def _sigmoid(x):
    return jax.nn.sigmoid(x)

def _layernorm(x, axis=-1, eps=1e-05):
    m = jnp.mean(x, axis=axis, keepdims=True)
    v = jnp.var(x, axis=axis, keepdims=True)
    return (x - m) / jnp.sqrt(v + eps)

def _scatter_add(tgt, idx, src, axis=0):
    return tgt.at[idx].add(src)

def _segment_sum(src, seg, n):
    return jax.ops.segment_sum(src, seg, n)
kernel_name = 'mk_macaron_d1_jaxref_r8_79c342'

def setup_inputs(seed: int=0):
    np.random.seed(seed)
    _w = jnp.asarray

    def _L0_attn_setup():
        import jax, jax.numpy as jnp
        import numpy as np
        D_MODEL = 256
        N_HEAD = 16
        HEAD_DIM = D_MODEL // N_HEAD
        SCALE = 1.0 / HEAD_DIM ** 0.5
        key = jax.random.key(seed)
        kx, kq, kk, kv, ko = jax.random.split(key, 5)
        std = 1.0 / np.sqrt(D_MODEL)
        return {'x': jax.random.normal(kx, (2, 256, D_MODEL), dtype=jnp.float32), 'w_q': jax.random.normal(kq, (D_MODEL, D_MODEL), dtype=jnp.float32) * std, 'w_k': jax.random.normal(kk, (D_MODEL, D_MODEL), dtype=jnp.float32) * std, 'w_v': jax.random.normal(kv, (D_MODEL, D_MODEL), dtype=jnp.float32) * std, 'w_o': jax.random.normal(ko, (D_MODEL, D_MODEL), dtype=jnp.float32) * std}
    _L0_attn_in = _L0_attn_setup()

    def _L0_ffn_setup():
        import jax, jax.numpy as jnp
        import numpy as np
        ALPHA = 1.702
        LIMIT = 7.0
        EPS = 1e-05
        TOP_K = 4
        key = jax.random.key(seed)
        ks = jax.random.split(key, 8)
        B, S, H, I, E = (2, 64, 256, 256, 16)
        return {'x': jax.random.normal(ks[0], (B, S, H), jnp.float32), 'norm_w': jnp.ones((H,), jnp.float32), 'gate_w': jax.random.normal(ks[1], (E, H), jnp.float32) * 0.02, 'gate_b': jax.random.normal(ks[2], (E,), jnp.float32) * 0.02, 'w1': jax.random.normal(ks[3], (E, 2 * I, H), jnp.float32) * 0.02, 'b1': jax.random.normal(ks[4], (E, 2 * I), jnp.float32) * 0.02, 'w2': jax.random.normal(ks[5], (E, H, I), jnp.float32) * 0.02, 'b2': jax.random.normal(ks[6], (E, H), jnp.float32) * 0.02}
    _L0_ffn_in = _L0_ffn_setup()
    _d = {'L0_attn_x': _L0_attn_in['x'], 'L0_attn_w_q': _L0_attn_in['w_q'], 'L0_attn_w_k': _L0_attn_in['w_k'], 'L0_attn_w_v': _L0_attn_in['w_v'], 'L0_attn_w_o': _L0_attn_in['w_o'], 'L0_ffn_norm_w': _L0_ffn_in['norm_w'], 'L0_ffn_gate_w': _L0_ffn_in['gate_w'], 'L0_ffn_gate_b': _L0_ffn_in['gate_b'], 'L0_ffn_w1': _L0_ffn_in['w1'], 'L0_ffn_b1': _L0_ffn_in['b1'], 'L0_ffn_w2': _L0_ffn_in['w2'], 'L0_ffn_b2': _L0_ffn_in['b2']}
    _x0 = _d['L0_attn_x']
    _d['L0_attn_x'] = jax.random.normal(jax.random.fold_in(jax.random.key(seed), 1), (8, 256, 256), dtype=_x0.dtype)
    del _x0
    return _d

def reference(L0_attn_x, L0_attn_w_q, L0_attn_w_k, L0_attn_w_v, L0_attn_w_o, L0_ffn_norm_w, L0_ffn_gate_w, L0_ffn_gate_b, L0_ffn_w1, L0_ffn_b1, L0_ffn_w2, L0_ffn_b2):

    def _L0_attn_ref(x, w_q, w_k, w_v, w_o):
        import jax, jax.numpy as jnp
        import numpy as np
        D_MODEL = 256
        N_HEAD = 16
        HEAD_DIM = D_MODEL // N_HEAD
        SCALE = 1.0 / HEAD_DIM ** 0.5
        b, s, d = x.shape

        def proj(w):
            y = jnp.einsum('bsd,ed->bse', x, w)
            return y.reshape(b, s, N_HEAD, HEAD_DIM).transpose(0, 2, 1, 3)
        q, k, v = (proj(w_q), proj(w_k), proj(w_v))
        scores = jnp.einsum('bhqd,bhkd->bhqk', q, k) * SCALE
        probs = jax.nn.softmax(scores, axis=-1)
        attn = jnp.einsum('bhqk,bhkd->bhqd', probs, v)
        attn = attn.transpose(0, 2, 1, 3).reshape(b, s, d)
        return jnp.einsum('bsd,ed->bse', attn, w_o)

    def _L0_ffn_ref(x, norm_w, gate_w, gate_b, w1, b1, w2, b2):
        import jax, jax.numpy as jnp
        import numpy as np
        ALPHA = 1.702
        LIMIT = 7.0
        EPS = 1e-05
        TOP_K = 4
        B, S, H = x.shape
        M = B * S
        E = gate_w.shape[0]
        xf = x.reshape(M, H)
        t = xf * jax.lax.rsqrt(jnp.mean(xf * xf, axis=-1, keepdims=True) + EPS) * norm_w
        logits = t @ gate_w.T + gate_b
        vals, idx = jax.lax.top_k(logits, TOP_K)
        gates_k = jax.nn.softmax(vals, axis=-1)
        G = jnp.zeros((M, E), x.dtype).at[jnp.arange(M)[:, None], idx].set(gates_k)
        h = jnp.einsum('mh,eoh->emo', t, w1) + b1[:, None, :]
        a = jnp.minimum(h[..., ::2], LIMIT)
        b = jnp.clip(h[..., 1::2], -LIMIT, LIMIT)
        act = a * jax.nn.sigmoid(ALPHA * a) * (b + 1.0)
        y = jnp.einsum('emi,edi->emd', act, w2) + b2[:, None, :]
        delta = jnp.einsum('me,emd->md', G, y)
        return x + delta.reshape(B, S, H)
    x = L0_attn_x
    x = x + 0.5 * _L0_ffn_ref(_layernorm(x, axis=-1), L0_ffn_norm_w, L0_ffn_gate_w, L0_ffn_gate_b, L0_ffn_w1, L0_ffn_b1, L0_ffn_w2, L0_ffn_b2)
    x = x + _L0_attn_ref(_layernorm(x, axis=-1), L0_attn_w_q, L0_attn_w_k, L0_attn_w_v, L0_attn_w_o)
    x = x + 0.5 * _L0_ffn_ref(_layernorm(x, axis=-1), L0_ffn_norm_w, L0_ffn_gate_w, L0_ffn_gate_b, L0_ffn_w1, L0_ffn_b1, L0_ffn_w2, L0_ffn_b2)
    return x

_drawn_inputs = setup_inputs


def setup_inputs(seed=0):
    import zlib

    import numpy as np

    out = dict(_drawn_inputs(seed))
    spreads = {'L0_ffn_norm_w': (1.0, 0.6)}
    factors = {'L0_ffn_gate_w': 3.421,
     'L0_ffn_gate_b': 8.0,
     'L0_ffn_w1': 3.177,
     'L0_ffn_b1': 8.0,
     'L0_ffn_w2': 3.085,
     'L0_ffn_b2': 8.0}
    for name, (base, spread) in spreads.items():
        noise = np.random.default_rng([zlib.crc32(name.encode()), seed]).standard_normal(out[name].shape)
        drawn = base * np.exp(spread * noise) if base else spread * noise
        out[name] = jnp.asarray(drawn.astype(out[name].dtype))
    for name, factor in factors.items():
        out[name] = (out[name] * factor).astype(out[name].dtype)
    return out
```

```python
import concourse.bass as bass
from concourse import mybir
from contextlib import ExitStack

fp32 = mybir.dt.float32
fp32r = mybir.dt.float32r
bf16 = mybir.dt.bfloat16
i32 = mybir.dt.int32
u32 = mybir.dt.uint32
ALU = mybir.AluOpType
ACT = mybir.ActivationFunctionType
X_AXIS = mybir.AxisListType.X

P = 128
B, S, D = 8, 256, 256
T = B * S
NE, TOP = 16, 4
I2, I1 = 512, 256
KC = D // P
WCOLS = KC * I2 + KC * D
BCOLS = I2 + D
REGION = T + P
NT = T * TOP // P + NE
ROWC = D + NE + 1
GPT = 2
NG = T // (GPT * P)
LIMIT, ALPHA, EPS = 7.0, 1.702, 1e-5
NH, HD = 16, 16
SCALE = HD ** -0.5


class Count:

    def __init__(self, sem, by=1):
        self.sem, self.by, self.n = sem, by, 0

    def inc(self, instruction):
        instruction.then_inc(self.sem, self.by)
        self.n += self.by
        return self.n


class Memory:

    def __init__(self, nc, stack, phase):
        self.nc, self.stack, self.phase, self.sems = nc, stack, phase, []
        stack.callback(self.clear)

    def clear(self):
        self.nc.clear_and_free_semaphores(self.sems)
        self.nc.all_engine_barrier()

    def sb(self, name, shape, dt):
        return self.stack.enter_context(self.nc.sbuf_tensor(f"{self.phase}_{name}", shape, dt))

    def ps(self, name, shape, dt=fp32):
        return self.stack.enter_context(self.nc.psum_tensor(f"{self.phase}_{name}", shape, dt))

    def sem(self, name):
        self.sems.append(self.nc.alloc_semaphore(f"{self.phase}_{name}"))
        return self.sems[-1]


def constants(nc, mem, norm_w, gate_wT, gate_b):
    c = {}
    c["ident"] = mem.sb("ident", [P, P], fp32)
    c["ones_r"] = mem.sb("ones_r", [P, P], fp32r)
    c["ones_b"] = mem.sb("ones_b", [P, P], bf16)
    c["before"] = mem.sb("before", [P, P], bf16)
    c["norm_w"] = mem.sb("norm_w", [P, D], fp32)
    c["gate_wT"] = mem.sb("gate_wT", [P, KC, NE], fp32)
    c["gate_b"] = mem.sb("gate_b", [P, GPT, NE], fp32)
    c["ramp_e"] = mem.sb("ramp_e", [P, NE], fp32)
    c["ramp_region"] = mem.sb("ramp_region", [P, NE], fp32)
    c["ramp_m"] = mem.sb("ramp_m", [P, T // P], fp32)
    c["ramp_t"] = mem.sb("ramp_t", [P, NT], fp32)
    c["token0"] = mem.sb("token0", [P, GPT], fp32)
    c["minus_half"] = mem.sb("minus_half", [P, GPT], fp32)
    c["one_e"] = mem.sb("one_e", [P, NE], fp32)
    c["pad"] = mem.sb("pad", [P, ROWC], fp32)
    c["zero"] = mem.sb("zero", [P, D], fp32)
    loaded, made, init, ones = (mem.sem(n) for n in ("loaded", "made", "init", "ones"))
    with nc.Block() as block:
        @block.sync
        def _(sp):
            sp.dma_start(c["norm_w"][:, :], norm_w.rearrange("(a d) -> a d", a=1).to_broadcast([P, D])).then_inc(loaded, 16)
            sp.dma_start(c["gate_wT"][:, :, :], gate_wT.rearrange("(c p) e -> p c e", p=P)).then_inc(loaded, 16)
            for g in range(GPT):
                sp.dma_start(c["gate_b"][:, g, :], gate_b.rearrange("(a e) -> a e", a=1).to_broadcast([P, NE])).then_inc(loaded, 16)
            sp.wait_ge(loaded, 16 * (2 + GPT))

        @block.gpsimd
        def _(pool):
            filled = [pool.memset(c["ident"][:, :], 0.0), pool.memset(c["before"][:, :], 1.0),
                      pool.memset(c["ones_b"][:, :], 1.0), pool.memset(c["pad"][:, :], 0.0),
                      pool.memset(c["zero"][:, :], 0.0), pool.memset(c["minus_half"][:, :], -0.5),
                      pool.memset(c["one_e"][:, :], 1.0)]
            for f in filled:
                f.then_inc(init, 1)
            pool.wait_ge(init, len(filled))
            pool.affine_select(out=c["ident"][:, :], in_=c["ident"][:, :], compare_op=ALU.not_equal, fill=1.0,
                               base=0, pattern=[[-1, P]], channel_multiplier=1).then_inc(made, 1)
            pool.affine_select(out=c["before"][:, :], in_=c["before"][:, :], compare_op=ALU.is_gt, fill=0.0,
                               base=0, pattern=[[1, P]], channel_multiplier=-1).then_inc(made, 1)
            approx = dict(allow_small_or_imprecise_dtypes=True)
            pool.iota(c["ramp_e"][:, :], pattern=[[1, NE]], base=0, channel_multiplier=0, **approx).then_inc(made, 1)
            pool.iota(c["ramp_region"][:, :], pattern=[[REGION, NE]], base=0, channel_multiplier=0, **approx).then_inc(made, 1)
            pool.iota(c["ramp_m"][:, :], pattern=[[P, T // P]], base=0, channel_multiplier=0, **approx).then_inc(made, 1)
            pool.iota(c["ramp_t"][:, :], pattern=[[1, NT]], base=0, channel_multiplier=0, **approx).then_inc(made, 1)
            pool.iota(c["token0"][:, :], pattern=[[P, GPT]], base=0, channel_multiplier=1, **approx).then_inc(made, 1)
            pool.iota(c["pad"][:, ROWC - 1:ROWC].bitcast(i32), pattern=[[1, 1]], base=T, channel_multiplier=1).then_inc(made, 1)
            pool.wait_ge(made, 8)

        @block.vector
        def _(dve):
            dve.memset(c["ones_r"][:, :].bitcast(fp32), 1.0).then_inc(ones, 1)
            dve.wait_ge(ones, 1)
    return c


class Chain:

    def __init__(self, engine, sem, turn=None, per=0):
        self.engine, self.sem, self.turn, self.per, self.n = engine, sem, turn, per, 0

    def done(self, instruction):
        instruction.then_inc(self.sem, 1)
        self.n += 1

    def after(self):
        self.engine.wait_ge(self.sem, self.n if self.turn is None else self.turn * self.per + self.n)

    def link(self, instruction):
        self.done(instruction)
        self.after()


def carry(engine, sem):
    engine.sem_inc(sem, 1)


def split_biases(nc, b_raw, b_split):
    with ExitStack() as stack:
        m = Memory(nc, stack, "bias")
        raw, part = m.sb("raw", [NE, BCOLS], fp32), m.sb("part", [NE, 2, BCOLS], fp32r)
        s_in, s_hi, s_lo, s_out = (m.sem(n) for n in ("in", "hi", "lo", "out"))
        with nc.Block() as block:
            @block.sync
            def _(sp):
                sp.dma_start(raw[:, :], b_raw).then_inc(s_in, 16)
                sp.wait_ge(s_lo, 1)
                sp.dma_start(b_split, part[:, :, :].bitcast(fp32)).then_inc(s_out, 16)
                sp.wait_ge(s_out, 16)

            @block.vector
            def _(dve):
                dve.wait_ge(s_in, 16)
                dve.tensor_copy(part[:, 0, :], raw[:, :]).then_inc(s_hi, 1)
                dve.wait_ge(s_hi, 1)
                dve.tensor_tensor(part[:, 1, :], raw[:, :], part[:, 0, :].bitcast(fp32), ALU.subtract).then_inc(s_lo, 1)


def route(nc, c, phase, x, table, rows, acc, weights=None):
    with ExitStack() as stack:
        m = Memory(nc, stack, phase)
        row = [m.sb(f"row{i}", [P, GPT, ROWC], fp32) for i in range(2)]
        slot_i = [m.sb(f"slot_i{i}", [P, GPT, TOP], i32) for i in range(2)]
        junk_a = m.sb("junk_a", [P, GPT, D], fp32)
        stats, mv = m.sb("stats", [P, GPT, 6], fp32), m.sb("mv", [P, GPT, 2], fp32)
        var, rstd = m.sb("var", [P, GPT], fp32), m.sb("rstd", [P, GPT], fp32)
        xn, junk = m.sb("xn", [P, GPT, D], fp32), m.sb("junk", [P, D], fp32)
        ms, mse, rms = (m.sb(n, [P, GPT], fp32) for n in ("ms", "mse", "rms"))
        tT = m.sb("tT", [P, GPT, KC, P], fp32)
        logit = m.sb("logit", [P, GPT, NE], fp32)
        top, topi = m.sb("top", [P, GPT, 8], fp32), m.sb("topi", [P, GPT, 8], u32)
        topf, diff, ex, gate, slot_k = (m.sb(n, [P, GPT, TOP], fp32) for n in ("topf", "diff", "ex", "gate", "slot_k"))
        den, rden = m.sb("den", [P, GPT], fp32), m.sb("rden", [P, GPT], fp32)
        hot, mix = m.sb("hot", [P, GPT, TOP, NE], fp32), m.sb("mix", [P, GPT, TOP, NE], fp32)
        sent = m.sb("sent", [P, GPT, NE], bf16)
        count, slot = m.sb("count", [P, NE], fp32), m.sb("slot", [P, GPT, NE], fp32)
        token = m.sb("token", [P, GPT], fp32)
        cnt, nt, tend, tbeg = (m.sb(n, [P, NE], fp32) for n in ("cnt", "nt", "tend", "tbeg"))
        more = m.sb("more", [P, NE, T // P], fp32)
        past, pastn = m.sb("past", [P, NT, NE], fp32), m.sb("pastn", [P, NT, NE], fp32)
        te, tn, off = (m.sb(n, [P, NT], fp32) for n in ("te", "tn", "off"))
        psT, psL, psR = m.ps("psT", [P, GPT, KC, P]), m.ps("psL", [P, GPT, NE]), m.ps("psR", [P, GPT + 1, NE])
        s_carry, s_carryp = m.sem("carry"), m.sem("carryp")
        s_v, s_vt = m.sem("v"), m.sem("vt")
        s_scat = [m.sem(f"scat{i}") for i in range(2)]
        (s_var, s_rstd, s_xn, s_ms, s_mse, s_rms, s_row, s_tp, s_tT, s_log, s_diff, s_ex, s_sent, s_rank,
         s_slot, s_all, s_tab, s_pad, s_zero) = (m.sem(n) for n in (
             "var", "rstd", "xn", "ms", "mse", "rms", "row", "tp", "tT", "log", "diff", "ex", "sent",
             "rank", "slot", "all", "tab", "pad", "zero"))
        s_x = m.sem("x")
        if weights:
            w_raw, w_split = weights
            wf = [m.sb(f"wf{k}", [P, WCOLS], fp32) for k in range(2)]
            ws = [m.sb(f"ws{k}", [P, 2, WCOLS], fp32r) for k in range(2)]
            s_wf, s_wh, s_wl, s_wo = ([m.sem(f"{n}{k}") for k in range(2)] for n in ("wf", "wh", "wl", "wo"))
        UN = 2
        PER = 26

        with nc.Block() as block:
            @block.sync
            def _(sp):
                if weights:
                    for s_ in s_wo:
                        sp.sem_inc(s_, 1)
                z = c["zero"][:, None, :].to_broadcast([P, T // P, D])
                sp.dma_start(acc[1][0:T, :].rearrange("(j p) d -> p j d", p=P), z).then_inc(s_zero, 16)
                sp.dma_start(acc[0][T:T + P, :], c["zero"][:, :]).then_inc(s_zero, 16)
                if weights:
                    for k in range(2):
                        sp.dma_start(wf[k][:, :], w_raw[k]).then_inc(s_wf[k], 16)

                    def store(g, k):
                        sp.wait_ge(s_wl[k], g + 1)
                        dst = w_split[bass.ds(2 * g + k, 1)].rearrange("a p h n -> (a p) h n")
                        sp.dma_start(dst, ws[k][:, :, :].bitcast(fp32)).then_inc(s_wo[k], 16)
                    with sp.Fori(0, NG - 1) as g:
                        for k in range(2):
                            store(g, k)
                            sp.dma_start(wf[k][:, :], w_raw[bass.ds(2 * g + (2 + k), 1)].rearrange("a p n -> (a p) n")).then_inc(s_wf[k], 16)
                    for k in range(2):
                        store(NG - 1, k)
                sp.wait_ge(s_all, 1)
                sp.dma_start(acc[0][0:T, :].rearrange("(j p) d -> p j d", p=P), x[:, :, :]).then_inc(s_zero, 16)
                sp.wait_ge(s_tab, 1)
                with sp.Fori(0, NE) as e:
                    at = sp.value_load(table[0:1, bass.ds(2 * NT + e, 1)], min_val=0, max_val=NE * REGION - P)
                    sp.dma_start(rows[bass.ds(at, P), :], c["pad"][:, :]).then_inc(s_pad, 16)
                sp.wait_ge(s_pad, 16 * NE)
                sp.wait_ge(s_zero, 16 * 3)
                if weights:
                    for k in range(2):
                        sp.wait_ge(s_wo[k], 16 * NG + 1)

            @block.vector
            def _(dve):
                for s_ in (s_slot,):
                    dve.sem_inc(s_, 1)
                one = Chain(dve, s_vt)
                one.done(dve.tensor_copy(count[:, :], c["ramp_region"][:, :]))
                one.link(dve.tensor_copy(token[:, :], c["token0"][:, :]))
                if weights:
                    def low(g, k):
                        dve.wait_ge(s_wh[k], g + 1)
                        dve.tensor_tensor(ws[k][:, 1, :], wf[k][:, :], ws[k][:, 0, :].bitcast(fp32), ALU.subtract).then_inc(s_wl[k], 1)
                with dve.Fori(0, NG // UN) as r:
                    ch = Chain(dve, s_v, r, UN * PER)
                    for i in range(UN):
                        g = r * UN + i
                        xv = x[:, bass.ds(g * GPT, GPT), :]
                        for t in range(GPT):
                            ch.done(dve.bn_stats(stats[:, t, :], xv[:, t, :]))
                        ch.after()
                        carry(dve, s_carry)
                        for t in range(GPT):
                            ch.done(dve.bn_aggr(mv[:, t, :], stats[:, t, :]))
                        ch.after()
                        dve.tensor_scalar(var[:, :], mv[:, :, 1], EPS, None, ALU.add).then_inc(s_var, 1)
                        dve.wait_ge(s_rstd, g + 1)
                        for t in range(GPT):
                            last = dve.tensor_scalar(xn[:, t, :], xv[:, t, :], mv[:, t, 0:1], rstd[:, t:t + 1], ALU.subtract, ALU.mult)
                            if t < GPT - 1:
                                ch.done(last)
                        last.then_inc(s_xn, 1)
                        dve.wait_ge(s_xn, g + 1)
                        ch.after()
                        ch.done(dve.scalar_tensor_tensor(xv, xn[:, :, :], 0.5, xv, ALU.mult, ALU.add))
                        if weights:
                            low(g, 0)
                        dve.wait_ge(s_ms, g + 1)
                        dve.tensor_scalar(mse[:, :], ms[:, :], EPS, None, ALU.add).then_inc(s_mse, 1)
                        dve.wait_ge(s_rms, g + 1)
                        dve.wait_ge(s_scat[i], 16 * GPT * TOP * r + 16)
                        for t in range(GPT):
                            last = dve.scalar_tensor_tensor(row[i][:, t, 0:D], xn[:, t, :], rms[:, t:t + 1], c["norm_w"][:, :], ALU.mult, ALU.mult)
                            if t < GPT - 1:
                                ch.done(last)
                        last.then_inc(s_row, 1)
                        ch.done(dve.tensor_copy(row[i][:, :, ROWC - 1].bitcast(i32), token[:, :]))
                        ch.after()
                        ch.done(dve.tensor_scalar(token[:, :], token[:, :], float(GPT * P), None, ALU.add))
                        if weights:
                            low(g, 1)
                        dve.wait_ge(s_log, g + 1)
                        ch.done(dve.tensor_tensor(logit[:, :, :], psL[:, :, :], c["gate_b"][:, :, :], ALU.add))
                        ch.after()
                        carry(dve, s_carry)
                        for t in range(GPT):
                            ch.done(dve.max(top[:, t, :], logit[:, t, :]))
                        ch.after()
                        dve.tensor_tensor(diff[:, :, :], top[:, :, 0:TOP], top[:, :, 0:1].to_broadcast([P, GPT, TOP]), ALU.subtract).then_inc(s_diff, 1)
                        for t in range(GPT):
                            ch.done(dve.max_index(topi[:, t, :], top[:, t, :], logit[:, t, :]))
                        ch.after()
                        ch.link(dve.tensor_copy(topf[:, :, :], topi[:, :, 0:TOP]))
                        full = [P, GPT, TOP, NE]
                        ch.link(dve.tensor_tensor(hot[:, :, :, :], c["ramp_e"][:, None, None, :].to_broadcast(full),
                                                  topf[:, :, :, None].to_broadcast(full), ALU.is_equal))
                        with nc.allow_low_precision("zeros and ones"):
                            dve.tensor_reduce(sent[:, :, :], hot[:, :, :, :].rearrange("p t k e -> p t e k"), X_AXIS, ALU.add).then_inc(s_sent, 1)
                        dve.wait_ge(s_ex, g + 1)
                        ch.link(dve.tensor_reduce(den[:, :], ex[:, :, :], X_AXIS, ALU.add))
                        ch.link(dve.tensor_scalar(den[:, :], den[:, :], 2.0, None, ALU.mult))
                        ch.link(dve.reciprocal(rden[:, :], den[:, :]))
                        ch.link(dve.tensor_tensor(gate[:, :, :], ex[:, :, :], rden[:, :, None].to_broadcast([P, GPT, TOP]), ALU.mult))
                        ch.link(dve.tensor_tensor(mix[:, :, :, :], hot[:, :, :, :], gate[:, :, :, None].to_broadcast(full), ALU.mult))
                        ch.link(dve.tensor_reduce(row[i][:, :, D:D + NE], mix[:, :, :, :].rearrange("p t k e -> p t e k"), X_AXIS, ALU.add))
                        dve.wait_ge(s_rank, g + 1)
                        ch.link(dve.tensor_tensor(slot[:, :, :], psR[:, 0:GPT, :], count[:, None, :].to_broadcast([P, GPT, NE]), ALU.add))
                        ch.done(dve.tensor_tensor(count[:, :], psR[:, GPT, :], count[:, :], ALU.add))
                        ch.link(dve.tensor_tensor(mix[:, :, :, :], hot[:, :, :, :], slot[:, :, None, :].to_broadcast(full), ALU.mult))
                        ch.link(dve.tensor_reduce(slot_k[:, :, :], mix[:, :, :, :], X_AXIS, ALU.add))
                        dve.tensor_copy(slot_i[i][:, :, :], slot_k[:, :, :]).then_inc(s_slot, 1)
                    assert ch.n == UN * PER, ch.n
                dve.wait_ge(s_v, NG * PER)
                one.done(dve.tensor_copy(junk[:, 0:1], count[:, 0:1]))
                dve.tensor_copy(junk[:, 1:2], c["zero"][:, 0:1]).then_inc(s_all, 1)
                one.link(dve.tensor_tensor(cnt[:, :], count[:, :], c["ramp_region"][:, :], ALU.subtract))
                shape = [P, NE, T // P]
                one.link(dve.tensor_tensor(more[:, :, :], cnt[:, :, None].to_broadcast(shape), c["ramp_m"][:, None, :].to_broadcast(shape), ALU.is_gt))
                one.link(dve.tensor_reduce(nt[:, :], more[:, :, :], X_AXIS, ALU.add))
                one.link(dve.tensor_scalar(nt[:, :], nt[:, :], 1.0, None, ALU.max))
                one.link(dve.tensor_tensor_scan(tend[:, :], c["one_e"][:, :], nt[:, :], 0.0, ALU.mult, ALU.add))
                one.link(dve.tensor_tensor(tbeg[:, :], tend[:, :], nt[:, :], ALU.subtract))
                shape = [P, NT, NE]
                one.link(dve.tensor_tensor(past[:, :, :], c["ramp_t"][:, :, None].to_broadcast(shape), tend[:, None, :].to_broadcast(shape), ALU.is_ge))
                one.done(dve.tensor_reduce(te[:, :], past[:, :, :], X_AXIS, ALU.add))
                one.link(dve.tensor_tensor(pastn[:, :, :], past[:, :, :], nt[:, None, :].to_broadcast(shape), ALU.mult))
                one.link(dve.tensor_reduce(tn[:, :], pastn[:, :, :], X_AXIS, ALU.add))
                one.link(dve.tensor_tensor(tn[:, :], c["ramp_t"][:, :], tn[:, :], ALU.subtract))
                one.link(dve.tensor_scalar(tn[:, :], tn[:, :], float(P), None, ALU.mult))
                one.link(dve.scalar_tensor_tensor(off[:, :], te[:, :], float(REGION), tn[:, :], ALU.mult, ALU.add))
                one.done(dve.tensor_scalar(table[:, 0:NT], off[:, :], float(NE * REGION), None, ALU.min))
                one.done(dve.tensor_scalar(table[:, NT:2 * NT], te[:, :], float(NE - 1), None, ALU.min))
                one.done(dve.tensor_copy(table[:, 2 * NT:2 * NT + NE], count[:, :]))
                one.done(dve.tensor_copy(table[:, 2 * NT + NE:2 * NT + 2 * NE], tbeg[:, :]))
                one.after()
                dve.tensor_copy(junk[:, 2:3], c["zero"][:, 0:1]).then_inc(s_tab, 1)

            @block.gpsimd
            def _(pool):
                pool.dma_start(rows[NE * REGION:NE * REGION + P, :], c["pad"][:, :]).then_inc(s_scat[0], 16)
                pool.dma_start(acc[1][T:T + P, :], c["zero"][:, :]).then_inc(s_scat[1], 16)
                with pool.Fori(0, NG // UN) as r:
                    for i in range(UN):
                        g = r * UN + i
                        pool.wait_ge(s_var, g + 1)
                        pool.tensor_tensor(rstd[:, :], var[:, :], c["minus_half"][:, :], ALU.pow).then_inc(s_rstd, 1)
                        pool.wait_ge(s_mse, g + 1)
                        pool.tensor_tensor(rms[:, :], mse[:, :], c["minus_half"][:, :], ALU.pow).then_inc(s_rms, 1)
                        pool.wait_ge(s_slot, g + 1 + 1)
                        carry(pool, s_carryp)
                        for t in range(GPT):
                            for k in range(TOP):
                                pool.indirect_dma_start(out=rows[:, :], out_offset=bass.IndirectOffsetOnAxis(ap=slot_i[i][:, t, k:k + 1], axis=0),
                                                        in_=row[i][:, t, :], in_offset=None).then_inc(s_scat[i], 16)
                for i in range(UN):
                    pool.wait_ge(s_scat[i], 16 * GPT * TOP * NG // UN + 16)

            @block.scalar
            def _(act):
                for s_ in (s_tT,):
                    act.sem_inc(s_, 1)
                def high(g, k):
                    act.wait_ge(s_wf[k], 16 * (g + 1))
                    act.wait_ge(s_wo[k], 16 * g + 1)
                    act.activation(ws[k][:, 0, :], wf[k][:, :], ACT.Copy).then_inc(s_wh[k], 1)
                with act.Fori(0, NG) as g:
                    act.wait_ge(s_xn, g + 1)
                    for t in range(GPT):
                        last = act.activation(junk_a[:, t, :], xn[:, t, :], ACT.Square, scale=D ** -0.5, accum_out=ms[:, t:t + 1])
                    last.then_inc(s_ms, 1)
                    if weights:
                        high(g, 0)
                    act.wait_ge(s_tp, g + 1)
                    act.activation(tT[:, :, :, :], psT[:, :, :, :], ACT.Copy).then_inc(s_tT, 1)
                    if weights:
                        high(g, 1)
                    act.wait_ge(s_diff, g + 1)
                    act.activation(ex[:, :, :], diff[:, :, :], ACT.Exp).then_inc(s_ex, 1)

            @block.tensor
            def _(pe):
                with pe.Fori(0, NG // UN) as r:
                    for i in range(UN):
                        g = r * UN + i
                        pe.wait_ge(s_row, g + 1)
                        pe.wait_ge(s_tT, g + 1)
                        for t in range(GPT):
                            for k in range(KC):
                                last = pe.transpose(psT[:, t, k, :], row[i][:, t, k * P:(k + 1) * P], c["ident"][:, :])
                        last.then_inc(s_tp, 1)
                        pe.wait_ge(s_tT, g + 1 + 1)
                        for t in range(GPT):
                            for k in range(KC):
                                last = pe.matmul(psL[:, t, :], tT[:, t, k, :], c["gate_wT"][:, k, :], start=k == 0, stop=k == KC - 1)
                        last.then_inc(s_log, 1)
                        pe.wait_ge(s_sent, g + 1)
                        pe.wait_ge(s_slot, g + 1)
                        for t in range(GPT):
                            for u in range(t + 1):
                                pe.matmul(psR[:, t, :], c["before"][:, :] if u == t else c["ones_b"][:, :], sent[:, u, :], start=u == 0, stop=u == t)
                        for u in range(GPT):
                            last = pe.matmul(psR[:, GPT, :], c["ones_b"][:, :], sent[:, u, :], start=u == 0, stop=u == GPT - 1)
                        last.then_inc(s_rank, 1)


def experts(nc, c, phase, table, rows, acc, w_split, b_split):
    UN, NBUF = 8, 4
    with ExitStack() as stack:
        m = Memory(nc, stack, phase)
        w = m.sb("w", [P, NBUF, 2, WCOLS], fp32r)
        bias = m.sb("bias", [P, NBUF, BCOLS], fp32r)
        tb = m.sb("tb", [P, UN, ROWC], fp32)
        th, tl = m.sb("th", [P, 2, D], fp32r), m.sb("tl", [P, 2, D], fp32r)
        am, bc, sg, ac = (m.sb(n, [P, 2, I1], fp32) for n in ("am", "bc", "sg", "ac"))
        ah, al = m.sb("ah", [P, 2, I1], fp32r), m.sb("al", [P, 2, I1], fp32r)
        ys = m.sb("ys", [P, 4, D], fp32)
        psT = [m.ps(f"psT{i}", [P, 512]) for i in range(2)]
        psH = [m.ps(f"psH{i}", [P, 512]) for i in range(2)]
        psA = m.ps("psA", [P, 512])
        psY = [m.ps(f"psY{i}", [P, 512]) for i in range(2)]
        s_carry = m.sem("carry")
        s_w = [m.sem(f"w{b}") for b in range(NBUF)]
        s_tb = [m.sem(f"tb{q}") for q in range(UN)]
        s_add = [m.sem(f"add{q}") for q in range(2)]
        (s_bz, s_ready, s_tT, s_th, s_tl, s_h, s_am, s_hfree, s_sg, s_u, s_ac, s_aT, s_ah, s_al, s_y, s_ys) = (m.sem(n) for n in (
            "bz", "ready", "tT", "th", "tl", "h", "am", "hfree", "sg", "u", "ac", "aT", "ah", "al", "y", "ys"))

        def steps(engine, first, last, lead, emit):
            begin, end = 1, (NT - lead) // UN
            for s in range(first, begin * UN):
                emit(s // UN, s % UN, s)
            with engine.Fori(begin, end) as r:
                for q in range(UN):
                    emit(r, q, None)
            for s in range(end * UN, last + 1):
                emit(s // UN, s % UN, s)

        def valid(number, ahead):
            return number is None or 0 <= number + ahead < NT

        def later(number, ahead, n):
            return number is None or number + ahead >= n

        def landed(r, o):
            return (r + (o // UN + 1)) * 16

        def added(r, o):
            return r * (16 * UN // 2) + 16 * (o // 2 + 2)

        with nc.Block() as block:
            @block.sync
            def _(sp):
                sp.wait_ge(s_bz, 1)
                AHEAD = 2

                def load(e, b):
                    sp.dma_start(w[:, b, :, :].bitcast(fp32), w_split[bass.ds(e, 1)].rearrange("a p h n -> (a p) h n")).then_inc(s_w[b], 16)
                    sp.dma_start(bias[0:2, b, :].bitcast(fp32), b_split[bass.ds(e, 1)].rearrange("a h n -> (a h) n")).then_inc(s_w[b], 16)

                def ready(e, b, nth):
                    sp.wait_ge(s_w[b], 32 * nth)
                    sp.sem_inc(s_ready, 1)

                def replace(e, b):
                    done = sp.value_load(table[0:1, bass.ds(e + (2 * NT + NE - AHEAD + 1), 1)], min_val=0, max_val=NT)
                    sp.wait_ge(s_y, done + 1)
                    load(e + AHEAD, b)
                for e in range(AHEAD):
                    load(e, e)
                for e in range(AHEAD):
                    ready(e, e, 1)
                    load(e + AHEAD, e + AHEAD)
                with sp.Fori(0, (NE - NBUF) // NBUF) as r:
                    for k in range(NBUF):
                        o = AHEAD + k
                        ready(r * NBUF + o, o % NBUF, r + (o // NBUF + 1))
                        replace(r * NBUF + o, (o + AHEAD) % NBUF)
                for e in range(NE - AHEAD, NE):
                    ready(e, e % NBUF, e // NBUF + 1)

            @block.tensor
            def _(pe):
                for s_ in (s_y,):
                    pe.sem_inc(s_, 1)
                def expert(i):
                    return pe.value_load(table[0:1, bass.ds(i + NT, 1)], min_val=0, max_val=NE - 1)

                def emit(r, q, number):
                    s = r * UN + q
                    if valid(number, 1):
                        i, b = s + 1, (q + 1) % 2
                        pe.wait_ge(s_tb[(q + 1) % UN], landed(r, q + 1))
                        if later(number, 1, 2):
                            pe.wait_ge(s_tl, i - 1)
                        for k in range(KC):
                            last = pe.transpose(psT[b][:, k * P:(k + 1) * P], tb[:, (q + 1) % UN, k * P:(k + 1) * P], c["ident"][:, :])
                        last.then_inc(s_tT, 1)
                    if valid(number, 0):
                        b = q % 2
                        e = expert(s)
                        buf = pe.snap(e % NBUF)
                        pe.wait_ge(s_ready, e + 1)
                        pe.wait_ge(s_tl, s + 1)
                        if later(number, 0, 2):
                            pe.wait_ge(s_hfree, s - 1)
                        out = psH[b][:, :]
                        pe.matmul(out, c["ones_r"][:, :], bias[:, bass.ds(buf, 1), 0:I2], start=True, stop=False)
                        for k in range(KC):
                            for left, h in ((th, 0), (th, 1), (tl, 0)):
                                last = pe.matmul(out, left[:, b, k * P:(k + 1) * P], w[:, bass.ds(buf, 1), h, k * I2:(k + 1) * I2],
                                                 start=False, stop=k == KC - 1 and left is tl)
                        last.then_inc(s_h, 1)
                    if valid(number, -2):
                        i, b = s - 2, q % 2
                        e = expert(i)
                        buf = pe.snap(e % NBUF)
                        pe.wait_ge(s_al, i + 1)
                        if later(number, -2, 2):
                            pe.wait_ge(s_ys, i - 1)
                        out = psY[b][:, 0:D]
                        pe.matmul(out, c["ones_r"][:, :], bias[:, bass.ds(buf, 1), I2:I2 + D], start=True, stop=False)
                        for k in range(KC):
                            for left, h in ((ah, 0), (ah, 1), (al, 0)):
                                o = KC * I2 + k * D
                                last = pe.matmul(out, left[:, b, k * P:(k + 1) * P], w[:, bass.ds(buf, 1), h, o:o + D],
                                                 start=False, stop=k == KC - 1 and left is al)
                        last.then_inc(s_y, 1)
                    if valid(number, -1):
                        i, b = s - 1, (q + 1) % 2
                        pe.wait_ge(s_ac, i + 1)
                        if later(number, -1, 1):
                            pe.wait_ge(s_al, i)
                        for k in range(KC):
                            last = pe.transpose(psA[:, k * P:(k + 1) * P], ac[:, b, k * P:(k + 1) * P], c["ident"][:, :])
                        last.then_inc(s_aT, 1)
                steps(pe, -1, NT + 1, 1, emit)

            @block.vector
            def _(dve):
                dve.memset(bias[:, :, :].bitcast(fp32), 0.0).then_inc(s_bz, 1)

                def emit(r, q, number):
                    s = r * UN + q
                    if valid(number, -1):
                        i, b = s - 1, (q + 1) % 2
                        dve.wait_ge(s_h, i + 1)
                        if later(number, -1, 2):
                            dve.wait_ge(s_sg, i - 1)
                        dve.tensor_scalar(am[:, b, :], psH[b][:, 0:I1], LIMIT, None, ALU.min).then_inc(s_am, 1)
                        dve.tensor_scalar(bc[:, b, :], psH[b][:, I1:I2], LIMIT, -LIMIT, ALU.min, ALU.max).then_inc(s_hfree, 1)
                        dve.wait_ge(s_am, i + 1)
                        dve.wait_ge(s_hfree, i + 1)
                        if later(number, -1, 2):
                            dve.wait_ge(s_aT, i - 1)
                        dve.scalar_tensor_tensor(bc[:, b, :], bc[:, b, :], 1.0, am[:, b, :], ALU.add, ALU.mult).then_inc(s_u, 1)
                    if valid(number, -2):
                        i, b = s - 2, q % 2
                        dve.wait_ge(s_ah, i + 1)
                        dve.tensor_tensor(al[:, b, :], psA[:, 0:I1], ah[:, b, :].bitcast(fp32), ALU.subtract).then_inc(s_al, 1)
                    if valid(number, -1):
                        i, b = s - 1, (q + 1) % 2
                        dve.wait_ge(s_u, i + 1)
                        dve.wait_ge(s_sg, i + 1)
                        dve.tensor_tensor(ac[:, b, :], bc[:, b, :], sg[:, b, :], ALU.mult).then_inc(s_ac, 1)
                    if valid(number, 1):
                        i, b = s + 1, (q + 1) % 2
                        dve.wait_ge(s_th, i + 1)
                        dve.tensor_tensor(tl[:, b, :], psT[b][:, 0:D], th[:, b, :].bitcast(fp32), ALU.subtract).then_inc(s_tl, 1)
                steps(dve, -1, NT + 1, 1, emit)

            @block.scalar
            def _(act):
                def emit(r, q, number):
                    s = r * UN + q
                    if valid(number, 3):
                        i, n = s + 3, (q + 3) % UN
                        if later(number, 3, UN):
                            act.wait_ge(s_add[n % 2], added(r, q + 3 - UN))
                        at = act.value_load(table[0:1, bass.ds(i, 1)], min_val=0, max_val=NE * REGION)
                        act.dma_start(tb[:, n, :], rows[bass.ds(at, P), :]).then_inc(s_tb[n], 16)
                    if valid(number, -1):
                        i, b = s - 1, (q + 1) % 2
                        act.wait_ge(s_am, i + 1)
                        if later(number, -1, 2):
                            act.wait_ge(s_ac, i - 1)
                        act.activation(sg[:, b, :], am[:, b, :], ACT.Sigmoid, scale=ALPHA).then_inc(s_sg, 1)
                    if valid(number, -3):
                        i, b, n = s - 3, (q + 1) % 2, (q - 3) % 4
                        e = act.value_load(table[0:1, bass.ds(i + NT, 1)], min_val=0, max_val=NE - 1)
                        act.wait_ge(s_y, i + 1 + 1)
                        if later(number, -3, 4):
                            act.wait_ge(s_add[n % 2], added(r, q - 3 - 4))
                        act.activation(ys[:, n, :], psY[b][:, 0:D], ACT.Copy, scale=tb[:, (q - 3) % UN, bass.ds(e + D, 1)]).then_inc(s_ys, 1)
                    if valid(number, -2):
                        i, b = s - 2, q % 2
                        act.wait_ge(s_aT, i + 1)
                        if later(number, -2, 2):
                            act.wait_ge(s_y, i - 1 + 1)
                        act.activation(ah[:, b, :], psA[:, 0:I1], ACT.Copy).then_inc(s_ah, 1)
                    if valid(number, 1):
                        i, b = s + 1, (q + 1) % 2
                        act.wait_ge(s_tT, i + 1)
                        if later(number, 1, 2):
                            act.wait_ge(s_h, i - 1)
                        act.activation(th[:, b, :], psT[b][:, 0:D], ACT.Copy).then_inc(s_th, 1)
                steps(act, -3, NT + 2, 3, emit)

            @block.gpsimd
            def _(pool):
                for q in range(2):
                    pool.dma_start(acc[q][T:T + P, :], c["zero"][:, :]).then_inc(s_add[q], 16)
                with pool.Fori(0, NT // UN) as r:
                    for q in range(UN):
                        pool.wait_ge(s_ys, r * UN + (q + 1))
                        pool.wait_ge(s_add[q % 2], r * (16 * UN // 2) + 16 * (q // 2 + 1))
                        carry(pool, s_carry)
                        pool.indirect_dma_start(out=acc[q % 2][:, :], out_offset=bass.IndirectOffsetOnAxis(ap=tb[:, q, ROWC - 1:ROWC].bitcast(i32), axis=0),
                                                in_=ys[:, q % 4, :], in_offset=None, compute_op=ALU.add).then_inc(s_add[q % 2], 16)
                for q in range(2):
                    pool.wait_ge(s_add[q], 16 * NT // 2 + 16)


def attention(nc, c, x, w_qkv, w_oT):
    scratch = [nc.dram_tensor(f"scratch{i}", (4, D, S), fp32, kind="Internal").ap() for i in range(2)]
    QT = S // P
    HP, HC = NH // 2, P // HD
    STEP = P + HD
    with ExitStack() as stack:
        m = Memory(nc, stack, "a")
        wf = m.sb("wf", [P, KC, 3 * D], fp32)
        wof = m.sb("wof", [P, KC, D], fp32)
        wp = m.sb("wp", [P, 2, KC, 3 * D], fp32r)
        wop = m.sb("wop", [P, 2, KC, D], fp32r)
        stats, mv = m.sb("stats", [P, QT, 6], fp32), m.sb("mv", [P, QT, 2], fp32)
        var, rstd = m.sb("var", [P, QT], fp32), m.sb("rstd", [P, QT], fp32)
        xn = m.sb("xn", [P, QT, D], fp32)
        xp = m.sb("xp", [P, 2, KC, S], fp32r)
        qk = m.sb("qk", [P, 2, 2, KC, S], fp32r)
        qs = [m.sb(f"qs{i}", [P, HP, S], fp32r) for i in range(2)]
        ks = [m.sb(f"ks{i}", [P, HP, S], fp32r) for i in range(2)]
        vz = [m.sb(f"vz{i}", [P, 2, QT, KC, HC * STEP], fp32r) for i in range(2)]
        nm = m.sb("nm", [P, 2, QT], fp32)
        p = m.sb("p", [P, 2, QT, S], fp32)
        pp = m.sb("pp", [P, 2, 2, QT, S], fp32r)
        den, rden = m.sb("den", [P, QT, NH], fp32), m.sb("rden", [P, QT, NH], fp32)
        rx = m.sb("rx", [P, QT, NH, HD], fp32)
        rn = m.sb("rn", [P, KC, S], fp32)
        at = m.sb("at", [P, KC, S], fp32)
        ap = m.sb("ap", [P, 2, KC, S], fp32r)
        psS = [m.ps(f"psS{i}", [P, QT, S]) for i in range(2)]
        psP = [m.ps(f"psP{i}", [P, QT, S]) for i in range(2)]
        psO = [m.ps(f"psO{i}", [P, 512]) for i in range(2)]
        psG = [m.ps(f"psG{i}", [P, 512]) for i in range(2)]
        s_w, s_wh, s_wl, s_vz = m.sem("w"), m.sem("wh"), m.sem("wl"), m.sem("vz")
        s_v, s_carry = m.sem("v"), m.sem("carry")
        (s_var, s_rstd, s_xn, s_xT, s_xh, s_xl, s_q, s_qh, s_ql, s_k, s_kh, s_kl, s_vv, s_vh, s_vl) = (m.sem(n) for n in (
            "var", "rstd", "xn", "xT", "xh", "xl", "q", "qh", "ql", "k", "kh", "kl", "vv", "vh", "vl"))
        s_st, s_ld = m.sem("st"), [m.sem(f"ld{i}") for i in range(2)]
        (s_s, s_nm, s_e, s_pT, s_ph, s_pl, s_pv, s_rx, s_n, s_rn, s_at, s_ah, s_al, s_f, s_x) = (m.sem(n) for n in (
            "s", "nm", "e", "pT", "ph", "pl", "pv", "rx", "n", "rn", "at", "ah", "al", "f", "x"))
        PER = 4

        def heads_of(vzb, part, t):
            return vzb[:, part, t, :, :].rearrange("p c (h s) -> p c h s", s=STEP)[:, :, :, 0:HD]

        with nc.Block() as block:
            @block.sync
            def _(sp):
                sp.dma_start(wf[:, :, :], w_qkv.rearrange("(c p) n -> p c n", p=P)).then_inc(s_w, 16)
                sp.dma_start(wof[:, :, :], w_oT.rearrange("(c p) n -> p c n", p=P)).then_inc(s_w, 16)

                def stack_heads(n, i):
                    for k, s_part in ((0, s_ql), (1, s_kl)):
                        sp.wait_ge(s_part, n + 1)
                        for h in range(2):
                            sp.dma_start(scratch[i][2 * k + h].rearrange("(c p) n -> p c n", p=P), qk[:, k, h, :, :].bitcast(fp32)).then_inc(s_st, 16)
                    sp.wait_ge(s_st, (n + 1) * 64)
                    sp.wait_ge(s_s, (0 if isinstance(n, int) else n * NH - NH) + 1)
                    for k, dst, parts in ((0, qs[i], (0, 1, 0, 1)), (1, ks[i], (0, 0, 1, 1))):
                        for q, part in enumerate(parts):
                            for odd in range(2):
                                src = scratch[i][2 * k + part].rearrange("(g two d) n -> two d g n", two=2, d=HD)[odd]
                                o = odd * (P // 2) + q * HD
                                sp.dma_start(dst[o:o + HD, :, :].bitcast(fp32), src).then_inc(s_ld[i], 16)
                stack_heads(0, 0)
                with sp.Fori(0, B // 2) as r:
                    stack_heads(r * 2 + 1, 1)
                    stack_heads(r * 2 + 2, 0)
                sp.wait_ge(s_ld[0], 256 * (B // 2 + 1))
                sp.wait_ge(s_ld[1], 256 * (B // 2))

            @block.gpsimd
            def _(pool):
                for i in range(2):
                    pool.memset(vz[i][:, :, :, :, :].bitcast(fp32), 0.0).then_inc(s_vz, 1)
                with pool.Fori(0, B + 1) as n:
                    pool.wait_ge(s_var, n + 1)
                    pool.tensor_tensor(rstd[:, :], var[:, :], c["minus_half"][:, :], ALU.pow).then_inc(s_rstd, 1)

            def prepare(n, i):
                def dve_norm(dve, ch, n_x):
                    xv = x[:, bass.ds(n_x * QT, QT), :]
                    for t in range(QT):
                        ch.done(dve.bn_stats(stats[:, t, :], xv[:, t, :]))
                    ch.after()
                    carry(dve, s_carry)
                    for t in range(QT):
                        ch.done(dve.bn_aggr(mv[:, t, :], stats[:, t, :]))
                    ch.after()
                    dve.tensor_scalar(var[:, :], mv[:, :, 1], EPS, None, ALU.add).then_inc(s_var, 1)
                    dve.wait_ge(s_rstd, n + 1)
                    dve.wait_ge(s_xT, n)
                    for t in range(QT):
                        dve.tensor_scalar(xn[:, t, :], xv[:, t, :], mv[:, t, 0:1], rstd[:, t:t + 1], ALU.subtract, ALU.mult).then_inc(s_xn, 1)

                def pe_xT(pe):
                    pe.wait_ge(s_xn, QT * n + QT)
                    pe.wait_ge(s_vl, n)
                    for t in range(QT):
                        for k in range(KC):
                            last = pe.transpose(psG[0][:, k * S + t * P:k * S + (t + 1) * P], xn[:, t, k * P:(k + 1) * P], c["ident"][:, :])
                    last.then_inc(s_xT, 1)

                def split(act_or_dve, low, src, dst, s_src, s_hi, s_lo, wait=None, scale=1.0):
                    e = act_or_dve
                    if not low:
                        e.wait_ge(s_src, n + 1)
                        for s_, v in wait or ():
                            e.wait_ge(s_, v)
                        e.activation(dst[0], src, ACT.Copy, scale=scale).then_inc(s_hi, 1)
                    else:
                        e.wait_ge(s_hi, n + 1)
                        e.scalar_tensor_tensor(dst[1], src, scale, dst[0].bitcast(fp32), ALU.mult, ALU.subtract).then_inc(s_lo, 1)
                flat = lambda a: a.rearrange("p c n -> p (c n)")
                parts = {
                    "x": (psG[0][:, :], [flat(xp[:, h]) for h in range(2)], s_xT, s_xh, s_xl),
                    "q": (psG[1][:, :], [flat(qk[:, 0, h]) for h in range(2)], s_q, s_qh, s_ql),
                    "k": (psG[0][:, :], [flat(qk[:, 1, h]) for h in range(2)], s_k, s_kh, s_kl),
                }
                waits = {"x": [(s_vv, n)], "q": [(s_st, n * 64)], "k": [(s_st, n * 64)]}

                def act_part(act, which):
                    src, dst, a, b, d = parts[which]
                    split(act, False, src, dst, a, b, d, waits[which], SCALE if which == "q" else 1.0)

                def dve_part(dve, which):
                    src, dst, a, b, d = parts[which]
                    split(dve, True, src, dst, a, b, d, None, SCALE if which == "q" else 1.0)

                def pe_qk(pe, which):
                    k0, bank, s_out = (0, 1, s_q) if which == "q" else (D, 0, s_k)
                    pe.wait_ge(s_xl, n + 1)
                    if which == "q":
                        pe.wait_ge(s_x, (0 if isinstance(n, int) else n - 1) + 1)
                    for o in range(KC):
                        for k in range(KC):
                            for wh, xh in ((0, 0), (0, 1), (1, 0)):
                                last = pe.matmul(psG[bank][:, o * S:(o + 1) * S], wp[:, wh, k, k0 + o * P:k0 + (o + 1) * P], xp[:, xh, k, :],
                                                 start=k == 0 and (wh, xh) == (0, 0), stop=k == KC - 1 and wh == 1)
                    last.then_inc(s_out, 1)

                def pe_v(pe):
                    pe.wait_ge(s_kl, n + 1)
                    for t in range(QT):
                        for k in range(KC):
                            for wh, xh in ((0, 0), (1, 0), (0, 1)):
                                last = pe.matmul(psG[0][:, t * D:(t + 1) * D], xp[:, xh, k, t * P:(t + 1) * P], wp[:, wh, k, 2 * D:3 * D],
                                                 start=k == 0 and (wh, xh) == (0, 0), stop=k == KC - 1 and xh == 1)
                    last.then_inc(s_vv, 1)

                def v_part(e, low):
                    if not low:
                        e.wait_ge(s_vv, n + 1)
                        e.wait_ge(s_vz, 2)
                        e.wait_ge(s_pv, (0 if isinstance(n, int) else n * NH - NH) + 1)
                    else:
                        e.wait_ge(s_vh, QT * n + QT)
                    for t in range(QT):
                        src = psG[0][:, t * D:(t + 1) * D].rearrange("p (c h d) -> p c h d", c=KC, d=HD)
                        if not low:
                            e.activation(heads_of(vz[i], 0, t), src, ACT.Copy).then_inc(s_vh, 1)
                        else:
                            last = e.tensor_tensor(heads_of(vz[i], 1, t), src, heads_of(vz[i], 0, t).bitcast(fp32), ALU.subtract)
                    if low:
                        last.then_inc(s_vl, 1)
                return dve_norm, pe_xT, act_part, dve_part, pe_qk, pe_v, v_part

            @block.tensor
            def _(pe):
                for s_ in (s_f, s_pv, s_n, s_s,):
                    pe.sem_inc(s_, 1)
                pe.wait_ge(s_wl, 2)

                def prep(n, i, stage):
                    _, pe_xT, _, _, pe_qk, pe_v, _ = prepare(n, i)
                    if stage == 0:
                        pe_xT(pe)
                    elif stage == 1:
                        pe_qk(pe, "q")
                        pe_qk(pe, "k")
                    elif stage == 2:
                        pe_v(pe)
                for stage in range(3):
                    prep(0, 0, stage)

                def scores(b, i, h):
                    if h == 0:
                        pe.wait_ge(s_ld[i], (b_half[0] + 1) * 256)
                    elif h >= 2:
                        pe.wait_ge(s_e, b * NH + h - 1)
                    o = (h % 2) * (P // 2)
                    for t in range(QT):
                        last = pe.matmul(psS[h % 2][:, t, :], qs[i][o:o + P // 2, h // 2, t * P:(t + 1) * P], ks[i][o:o + P // 2, h // 2, :], start=True, stop=True)
                    last.then_inc(s_s, 1)

                def transposes(b, h):
                    pe.wait_ge(s_e, b * NH + h + 1)
                    if h >= 2:
                        pe.wait_ge(s_pl, b * NH + h - 1)
                    for q in range(QT):
                        for k in range(QT):
                            last = pe.transpose(psP[h % 2][:, k, q * P:(q + 1) * P], p[:, h % 2, q, k * P:(k + 1) * P], c["ident"][:, :])
                    last.then_inc(s_pT, 1)

                def values(b, i, h):
                    cc, hh = h // HC, h % HC
                    pe.wait_ge(s_pl, b * NH + h + 1)
                    if hh == 0:
                        pe.wait_ge(s_at, KC * b + 1)
                    for k in range(QT):
                        for vh, ph in ((0, 0), (1, 0), (0, 1)):
                            last = pe.matmul(psO[cc][:, 0:S], vz[i][:, vh, k, cc, hh * P:(hh + 1) * P], pp[:, h % 2, ph, k, :],
                                             start=hh == 0 and k == 0 and (vh, ph) == (0, 0), stop=hh == HC - 1 and k == QT - 1 and ph == 1)
                    last.then_inc(s_pv, 1)
                b_half = [0]

                def batch(r, i):
                    b = r * 2 + i
                    b_half[0] = r
                    scores(b, i, 0)
                    for h in range(NH):
                        if h < NH - 1:
                            scores(b, i, h + 1)
                        transposes(b, h)
                        if h:
                            values(b, i, h - 1)
                        if h in (3, 6, 9):
                            prep(b + 1, 1 - i, (3, 6, 9).index(h))
                    values(b, i, NH - 1)
                    pe.wait_ge(s_rx, b + 1 + 1)
                    pe.wait_ge(s_ql, b + 2)
                    for k in range(KC):
                        for t in range(QT):
                            last = pe.transpose(psG[1][:, k * S + t * P:k * S + (t + 1) * P], rx[:, t, k * HC:(k + 1) * HC, :].rearrange("p h d -> p (h d)"), c["ident"][:, :])
                    last.then_inc(s_n, 1)
                    pe.wait_ge(s_al, b + 1)
                    for t in range(QT):
                        for k in range(KC):
                            for a, wo in ((0, 0), (0, 1), (1, 0)):
                                last = pe.matmul(psG[1][:, t * D:(t + 1) * D], ap[:, a, k, t * P:(t + 1) * P], wop[:, wo, k, :],
                                                 start=k == 0 and (a, wo) == (0, 0), stop=k == KC - 1 and a == 1)
                    last.then_inc(s_f, 1)
                with pe.Fori(0, B // 2) as r:
                    for i in range(2):
                        batch(r, i)

            @block.vector
            def _(dve):
                for s_ in (s_at, s_rx, s_x,):
                    dve.sem_inc(s_, 1)
                dve.wait_ge(s_wh, 2)
                dve.tensor_tensor(wp[:, 1, :, :], wf[:, :, :], wp[:, 0, :, :].bitcast(fp32), ALU.subtract).then_inc(s_wl, 1)
                dve.tensor_tensor(wop[:, 1, :, :], wof[:, :, :], wop[:, 0, :, :].bitcast(fp32), ALU.subtract).then_inc(s_wl, 1)

                def prep(n, i, stage, ch, n_x):
                    dve_norm, _, _, dve_part, _, _, v_part = prepare(n, i)
                    if stage == 0:
                        dve_norm(dve, ch, n_x)
                    elif stage in (1, 2, 3):
                        dve_part(dve, "xqk"[stage - 1])
                    elif stage == 4:
                        v_part(dve, True)
                first = Chain(dve, s_v)
                for stage in range(5):
                    prep(0, 0, stage, first, 0)

                def maximum(b, h):
                    dve.wait_ge(s_s, b * NH + h + 1 + 1)
                    if h >= 2:
                        dve.wait_ge(s_e, b * NH + h - 1)
                    dve.tensor_reduce(nm[:, h % 2, :], psS[h % 2][:, :, :], X_AXIS, ALU.max, negate=True).then_inc(s_nm, 1)

                def low(b, h):
                    dve.wait_ge(s_ph, b * NH + h + 1)
                    dve.tensor_tensor(pp[:, h % 2, 1, :, :], psP[h % 2][:, :, :], pp[:, h % 2, 0, :, :].bitcast(fp32), ALU.subtract).then_inc(s_pl, 1)
                stage_at = {2: 0, 4: 1, 7: 2, 8: 3, 10: 4}

                def batch(r, i, ch):
                    b = r * 2 + i
                    maximum(b, 0)
                    for h in range(NH):
                        if h < NH - 1:
                            maximum(b, h + 1)
                        low(b, h)
                        if h in stage_at:
                            n_x = dve.snap((b + 1) % B)
                            prep(b + 1, 1 - i, stage_at[h], ch, n_x)
                    dve.wait_ge(s_e, NH * b + NH)
                    ch.link(dve.reciprocal(rden[:, :, :], den[:, :, :]))
                    dve.wait_ge(s_n, b + 1)
                    dve.tensor_copy(rx[:, :, :, :], rden[:, :, :, None].to_broadcast([P, QT, NH, HD])).then_inc(s_rx, 1)
                    dve.wait_ge(s_rn, b + 1)
                    dve.wait_ge(s_pv, NH * b + NH + 1)
                    for k in range(KC):
                        dve.tensor_tensor(at[:, k, :], psO[k][:, 0:S], rn[:, k, :], ALU.mult).then_inc(s_at, 1)
                    dve.wait_ge(s_ah, b + 1)
                    dve.tensor_tensor(ap[:, 1, :, :], at[:, :, :], ap[:, 0, :, :].bitcast(fp32), ALU.subtract).then_inc(s_al, 1)
                    dve.wait_ge(s_f, b + 1 + 1)
                    xv = x[:, bass.ds(b * QT, QT), :].rearrange("p t d -> p (t d)")
                    dve.tensor_tensor(xv, psG[1][:, :], xv, ALU.add).then_inc(s_x, 1)
                with dve.Fori(0, B // 2) as r:
                    ch = Chain(dve, s_v, r, 2 * (PER + 1))
                    ch.n = PER
                    for i in range(2):
                        batch(r, i, ch)
                    assert ch.n == PER + 2 * (PER + 1), ch.n

            @block.scalar
            def _(act):
                act.wait_ge(s_w, 32)
                act.activation(wp[:, 0, :, :], wf[:, :, :], ACT.Copy).then_inc(s_wh, 1)
                act.activation(wop[:, 0, :, :], wof[:, :, :], ACT.Copy).then_inc(s_wh, 1)

                def prep(n, i, stage):
                    _, _, act_part, _, _, _, v_part = prepare(n, i)
                    if stage < 3:
                        act_part(act, "xqk"[stage])
                    else:
                        v_part(act, False)
                for stage in range(4):
                    prep(0, 0, stage)

                def exponentials(b, h):
                    act.wait_ge(s_nm, b * NH + h + 1)
                    if h >= 2:
                        act.wait_ge(s_pT, b * NH + h - 1)
                    if h == 0:
                        act.wait_ge(s_rx, b + 1)
                    for t in range(QT):
                        last = act.activation(p[:, h % 2, t, :], psS[h % 2][:, t, :], ACT.Exp, bias=nm[:, h % 2, t:t + 1], accum_out=den[:, t, h:h + 1])
                    last.then_inc(s_e, 1)

                def high(b, h):
                    act.wait_ge(s_pT, b * NH + h + 1)
                    act.wait_ge(s_pv, b * NH + h - 1 + 1) if h >= 2 else None
                    act.activation(pp[:, h % 2, 0, :, :], psP[h % 2][:, :, :], ACT.Copy).then_inc(s_ph, 1)
                stage_at = {4: 0, 7: 1, 8: 2, 10: 3}

                def batch(r, i):
                    b = r * 2 + i
                    exponentials(b, 0)
                    for h in range(NH):
                        high(b, h)
                        if h < NH - 1:
                            exponentials(b, h + 1)
                        if h in stage_at:
                            prep(b + 1, 1 - i, stage_at[h])
                    act.wait_ge(s_n, b + 1 + 1)
                    act.wait_ge(s_at, KC * b + 1)
                    act.activation(rn[:, :, :].rearrange("p c n -> p (c n)"), psG[1][:, :], ACT.Copy).then_inc(s_rn, 1)
                    act.wait_ge(s_at, KC * b + KC + 1)
                    act.wait_ge(s_f, b + 1)
                    act.activation(ap[:, 0, :, :], at[:, :, :], ACT.Copy).then_inc(s_ah, 1)
                with act.Fori(0, B // 2) as r:
                    for i in range(2):
                        batch(r, i)


def gather(nc, c, phase, x, acc, out=None):
    with ExitStack() as stack:
        m = Memory(nc, stack, phase)
        part = m.sb("part", [P, T // P, D], fp32)
        NQ = 4
        s_in, s_sum, s_out = [m.sem(f"in{q}") for q in range(NQ)], m.sem("sum"), m.sem("out")
        n = T // P // NQ
        view = lambda a: a[0:T, :].rearrange("(j p) d -> p j d", p=P)
        with nc.Block() as block:
            @block.sync
            def _(sp):
                for q in range(NQ):
                    sp.dma_start(x[:, q * n:(q + 1) * n, :], view(acc[0])[:, q * n:(q + 1) * n, :]).then_inc(s_in[q], 16)
                    sp.dma_start(part[:, q * n:(q + 1) * n, :], view(acc[1])[:, q * n:(q + 1) * n, :]).then_inc(s_in[q], 16)
                if out is not None:
                    for q in range(NQ):
                        sp.wait_ge(s_sum, q + 1)
                        sp.dma_start(view(out)[:, q * n:(q + 1) * n, :], x[:, q * n:(q + 1) * n, :]).then_inc(s_out, 16)
                    sp.wait_ge(s_out, 16 * NQ)

            @block.vector
            def _(dve):
                for q in range(NQ):
                    dve.wait_ge(s_in[q], 32)
                    dve.tensor_tensor(x[:, q * n:(q + 1) * n, :], x[:, q * n:(q + 1) * n, :], part[:, q * n:(q + 1) * n, :], ALU.add).then_inc(s_sum, 1)
                dve.wait_ge(s_sum, NQ)


def load_tokens(nc, x, x_in):
    with ExitStack() as stack:
        m = Memory(nc, stack, "load")
        s = m.sem("x")
        with nc.Block() as block:
            @block.sync
            def _(sp):
                sp.dma_start(x[:, :, :], x_in.rearrange("(j p) d -> p j d", p=P)).then_inc(s, 16)
                sp.wait_ge(s, 16)


def store_tokens(nc, x, out):
    with ExitStack() as stack:
        m = Memory(nc, stack, "store")
        s = m.sem("x")
        with nc.Block() as block:
            @block.sync
            def _(sp):
                sp.dma_start(out.rearrange("(j p) d -> p j d", p=P), x[:, :, :]).then_inc(s, 16)
                sp.wait_ge(s, 16)


def build(nc, x_in, norm_w, gate_wT, gate_b, w_raw, b_raw, w_qkv, w_oT, out, attn=True, second=True):
    rows = nc.dram_tensor("rows", (NE * REGION + P, ROWC), fp32, kind="Internal").ap()
    acc = [[nc.dram_tensor(f"acc{f}{i}", (T + P, D), fp32, kind="Internal").ap() for i in range(2)] for f in range(2)]
    w_split = nc.dram_tensor("w_split", (NE, P, 2, WCOLS), fp32, kind="Internal").ap()
    b_split = nc.dram_tensor("b_split", (NE, 2, BCOLS), fp32, kind="Internal").ap()
    with ExitStack() as stack:
        mem = Memory(nc, stack, "all")
        x = mem.sb("x", [P, T // P, D], fp32)
        table = mem.sb("table", [P, 2 * NT + 2 * NE], i32)
        c = constants(nc, mem, norm_w, gate_wT, gate_b)
        load_tokens(nc, x, x_in)
        split_biases(nc, b_raw, b_split)
        route(nc, c, "r1", x, table, rows, acc[0], weights=(w_raw, w_split))
        experts(nc, c, "e1", table, rows, acc[0], w_split, b_split)
        gather(nc, c, "g1", x, acc[0], None if (attn or second) else out)
        if attn:
            attention(nc, c, x, w_qkv, w_oT)
            if not second:
                store_tokens(nc, x, out)
        if second:
            route(nc, c, "r2", x, table, rows, acc[1])
            experts(nc, c, "e2", table, rows, acc[1], w_split, b_split)
            gather(nc, c, "g2", x, acc[1], out)


def kernel(L0_attn_x, L0_attn_w_q, L0_attn_w_k, L0_attn_w_v, L0_attn_w_o, L0_ffn_norm_w, L0_ffn_gate_w,
           L0_ffn_gate_b, L0_ffn_w1, L0_ffn_b1, L0_ffn_w2, L0_ffn_b2):
    import numpy as np
    import concourse.bacc as bacc
    from concourse.bass_utils import run_bass_kernel_spmd

    arrays = layout(L0_attn_x, L0_attn_w_q, L0_attn_w_k, L0_attn_w_v, L0_attn_w_o, L0_ffn_norm_w, L0_ffn_gate_w,
                    L0_ffn_gate_b, L0_ffn_w1, L0_ffn_b1, L0_ffn_w2, L0_ffn_b2)
    nc = bacc.Bacc("TRN2", target_bir_lowering=False, num_devices=1)
    ins = [nc.dram_tensor(n, a.shape, fp32, kind="ExternalInput").ap() for n, a in arrays.items()]
    out = nc.dram_tensor("out", (T, D), fp32, kind="ExternalOutput").ap()
    build(nc, *ins, out)
    r = run_bass_kernel_spmd(nc, [arrays], core_ids=[0])
    return r.results[0]["out"].reshape(B, S, D)


def layout(x, w_q, w_k, w_v, w_o, norm_w, gate_w, gate_b, w1, b1, w2, b2):
    import numpy as np
    c = lambda a: np.ascontiguousarray(a)
    x, w_q, w_k, w_v, w_o, norm_w, gate_w, gate_b, w1, b1, w2, b2 = (
        np.asarray(a) for a in (x, w_q, w_k, w_v, w_o, norm_w, gate_w, gate_b, w1, b1, w2, b2))
    w1T = np.concatenate([w1[:, 0::2, :], w1[:, 1::2, :]], axis=1).transpose(0, 2, 1)
    w2T = w2.transpose(0, 2, 1)
    by_p = lambda a: a.reshape(NE, KC, P, -1).transpose(0, 2, 1, 3).reshape(NE, P, -1)
    return {
        "x_in": c(x.reshape(T, D)),
        "norm_w": c(norm_w),
        "gate_wT": c(gate_w.T),
        "gate_b": c(gate_b),
        "w_raw": c(np.concatenate([by_p(w1T), by_p(w2T)], axis=2)),
        "b_raw": c(np.concatenate([b1[:, 0::2], b1[:, 1::2], b2], axis=1)),
        "w_qkv": c(np.concatenate([w_q.T, w_k.T, w_v.T], axis=1)),
        "w_oT": c(w_o.T),
    }
```
